# Optimizing a Trainium2 kernel written in Bass

```python
import numpy as np
import jax
import jax.numpy as jnp

def _softmax(x, axis=-1):
    return jax.nn.softmax(x, axis=axis)

def _gelu(x):
    return jax.nn.gelu(x, approximate=True)

def _silu(x):
    return jax.nn.silu(x)

def _sigmoid(x):
    return jax.nn.sigmoid(x)

def _layernorm(x, axis=-1, eps=1e-05):
    m = jnp.mean(x, axis=axis, keepdims=True)
    v = jnp.var(x, axis=axis, keepdims=True)
    return (x - m) / jnp.sqrt(v + eps)

def _scatter_add(tgt, idx, src, axis=0):
    return tgt.at[idx].add(src)

def _segment_sum(src, seg, n):
    return jax.ops.segment_sum(src, seg, n)
kernel_name = 'mk_flamingo_gated_d1_seqx_r4_5ec092'

def setup_inputs(seed: int=0):
    np.random.seed(seed)
    _w = jnp.asarray

    def _rec_inputs():
        import jax
        import jax.numpy as jnp
        _rk = jax.random.key(seed)
        x = -0.0002928 + 1 * jax.random.normal(jax.random.fold_in(_rk, 1), (4, 512, 512), jnp.float32)
        _lenS = 512 - jax.random.randint(jax.random.fold_in(_rk, 7), (4,), 0, max(1, 512 // 4) + 1, jnp.int32)
        _lenS2 = 512 - jax.random.randint(jax.random.fold_in(_rk, 8), (4,), 0, max(1, 512 // 4) + 1, jnp.int32)
        _ctx_2048P = jax.random.normal(jax.random.fold_in(_rk, 11), (4, 16, 512), jnp.float32)
        _ctx_2048c = jax.random.dirichlet(jax.random.fold_in(_rk, 511), 0.3 * jnp.ones((16,), jnp.float32), (4, 512))
        _ctx_2048t = jnp.einsum('bsk,bkd->bsd', _ctx_2048c, _ctx_2048P)
        _ctx_2048t = _ctx_2048t * jax.lax.rsqrt(jnp.mean(jnp.square(_ctx_2048t)) + 1e-12) * 0.953939
        ctx_2048 = -1.39393e-06 + 0.999914 * (_ctx_2048t + 0.3 * jax.random.normal(jax.random.fold_in(_rk, 611), (4, 512, 512), jnp.float32))
        _validS = jnp.arange(512)[None, :] < _lenS[:, None]
        _validS2 = jnp.arange(512)[None, :] < _lenS2[:, None]
        _causal = jnp.tril(jnp.ones((512, 512), dtype=bool))
        mask_BxS2_if1 = jnp.where(jnp.ones((4, 512), dtype=bool), 1, 0).astype(jnp.int32)
        _g = jax.random.normal(jax.random.fold_in(_rk, 9001), (2, 1), jnp.float32)
        _g = jnp.sign(_g) * jnp.maximum(jnp.abs(_g), 1.0) + (_g == 0) * 1.0
        g_xattn = _g[0]
        g_ffn = _g[1]
        return (x, ctx_2048, mask_BxS2_if1, g_xattn, g_ffn)
    x, ctx_2048, mask_BxS2_if1, g_xattn, g_ffn = _rec_inputs()

    def _L0_xattn_setup():
        import jax, jax.numpy as jnp
        import numpy as np
        D_MODEL = 512
        N_HEADS = 32
        N_GROUPS = 8
        HEAD_DIM = D_MODEL // N_HEADS
        BATCH, SEQ = (2, 256)
        NEG_INF = float('-inf')
        key = jax.random.key(seed)
        ks = jax.random.split(key, 9)
        s = 0.02
        return {'Q': jax.random.normal(ks[0], (BATCH, SEQ, D_MODEL), jnp.float32), 'K': jax.random.normal(ks[1], (BATCH, SEQ, D_MODEL), jnp.float32), 'V': jax.random.normal(ks[2], (BATCH, SEQ, D_MODEL), jnp.float32), 'attention_mask': jnp.ones((BATCH, SEQ), jnp.int32), 'w_q': jax.random.normal(ks[3], (D_MODEL, D_MODEL), jnp.float32) * s, 'w_k': jax.random.normal(ks[4], (HEAD_DIM * N_GROUPS, D_MODEL), jnp.float32) * s, 'w_v': jax.random.normal(ks[5], (HEAD_DIM * N_GROUPS, D_MODEL), jnp.float32) * s, 'w_o': jax.random.normal(ks[6], (D_MODEL, D_MODEL), jnp.float32) * s, 'b_o': jnp.zeros((D_MODEL,), jnp.float32)}
    _L0_xattn_all = _L0_xattn_setup()
    _L0_xattn_in = {k: v for k, v in _L0_xattn_all.items() if k in ('w_q', 'w_k', 'w_v', 'w_o', 'b_o')}
    del _L0_xattn_all

    def _L0_ffn_setup():
        import jax, jax.numpy as jnp
        import numpy as np
        DIM = 512
        INTER = 352
        E = 16
        TOPK = 4
        G = 4
        TOPK_G = 2
        N_SHARED = 2
        SHARED_INTER = N_SHARED * INTER
        ROUTE_SCALE = 1.0

        def _moe_forward(x, Wg, W1, W3, W2, Ws1, Ws3, Ws2):
            B, S, D = x.shape
            xt = x.reshape(-1, D)
            T = xt.shape[0]
            scores = jax.nn.softmax(xt @ Wg.T, axis=-1)
            sg = scores.reshape(T, G, E // G)
            group_scores = sg.max(axis=-1)
            gidx = jax.lax.top_k(group_scores, TOPK_G)[1]
            gmask = jax.nn.one_hot(gidx, G, dtype=jnp.float32).sum(axis=1) > 0
            masked = jnp.where(gmask[:, :, None], sg, -jnp.inf).reshape(T, E)
            topi = jax.lax.top_k(masked, TOPK)[1]
            weights = jnp.take_along_axis(scores, topi, axis=1) * ROUTE_SCALE
            combine = jnp.zeros((T, E), xt.dtype).at[jnp.arange(T)[:, None], topi].add(weights)
            h = jax.nn.silu(jnp.einsum('td,eid->eti', xt, W1)) * jnp.einsum('td,eid->eti', xt, W3)
            expert_out = jnp.einsum('eti,edi->etd', h, W2)
            y = jnp.einsum('etd,te->td', expert_out, combine)
            z = jax.nn.silu(xt @ Ws1.T) * (xt @ Ws3.T) @ Ws2.T
            return (y + z).reshape(B, S, D)
        key = jax.random.key(seed)
        ks = jax.random.split(key, 8)
        s = 0.02
        x = jax.random.normal(ks[0], (1, 512, DIM), dtype=jnp.float32)
        Wg = jax.random.normal(ks[1], (E, DIM), dtype=jnp.float32) * s
        W1 = jax.random.normal(ks[2], (E, INTER, DIM), dtype=jnp.float32) * s
        W3 = jax.random.normal(ks[3], (E, INTER, DIM), dtype=jnp.float32) * s
        W2 = jax.random.normal(ks[4], (E, DIM, INTER), dtype=jnp.float32) * s
        Ws1 = jax.random.normal(ks[5], (SHARED_INTER, DIM), dtype=jnp.float32) * s
        Ws3 = jax.random.normal(ks[6], (SHARED_INTER, DIM), dtype=jnp.float32) * s
        Ws2 = jax.random.normal(ks[7], (DIM, SHARED_INTER), dtype=jnp.float32) * s
        return {'x': x, 'Wg': Wg, 'W1': W1, 'W3': W3, 'W2': W2, 'Ws1': Ws1, 'Ws3': Ws3, 'Ws2': Ws2}
    _L0_ffn_all = _L0_ffn_setup()
    _L0_ffn_in = {k: v for k, v in _L0_ffn_all.items() if k in ('Wg', 'W1', 'W3', 'W2', 'Ws1', 'Ws3', 'Ws2')}
    del _L0_ffn_all
    return {'x': x, 'ctx_2048': ctx_2048, 'mask_BxS2_if1': mask_BxS2_if1, 'g_xattn': g_xattn, 'g_ffn': g_ffn, 'L0_xattn_w_q': _L0_xattn_in['w_q'], 'L0_xattn_w_k': _L0_xattn_in['w_k'], 'L0_xattn_w_v': _L0_xattn_in['w_v'], 'L0_xattn_w_o': _L0_xattn_in['w_o'], 'L0_xattn_b_o': _L0_xattn_in['b_o'], 'L0_ffn_Wg': _L0_ffn_in['Wg'], 'L0_ffn_W1': _L0_ffn_in['W1'], 'L0_ffn_W3': _L0_ffn_in['W3'], 'L0_ffn_W2': _L0_ffn_in['W2'], 'L0_ffn_Ws1': _L0_ffn_in['Ws1'], 'L0_ffn_Ws3': _L0_ffn_in['Ws3'], 'L0_ffn_Ws2': _L0_ffn_in['Ws2']}

def reference(x, ctx_2048, mask_BxS2_if1, g_xattn, g_ffn, L0_xattn_w_q, L0_xattn_w_k, L0_xattn_w_v, L0_xattn_w_o, L0_xattn_b_o, L0_ffn_Wg, L0_ffn_W1, L0_ffn_W3, L0_ffn_W2, L0_ffn_Ws1, L0_ffn_Ws3, L0_ffn_Ws2):
    import jax
    import jax.numpy as jnp

    def _L0_xattn_ref(Q, K, V, attention_mask, w_q, w_k, w_v, w_o, b_o):
        import jax, jax.numpy as jnp
        import numpy as np
        D_MODEL = 512
        N_HEADS = 32
        N_GROUPS = 8
        HEAD_DIM = D_MODEL // N_HEADS
        BATCH, SEQ = (2, 256)
        NEG_INF = float('-inf')
        B, S, D = Q.shape
        G, HG, HD = (N_GROUPS, N_HEADS // N_GROUPS, HEAD_DIM)
        q = (Q @ w_q.T).reshape(B, S, G, HG, HD)
        k = (K @ w_k.T).reshape(B, S, G, HD)
        v = (V @ w_v.T).reshape(B, S, G, HD)
        scale = jnp.sqrt(jnp.float32(HD))
        scores = jnp.einsum('bnghd,bmgd->bnghm', q, k) / scale
        pad = (attention_mask == 0)[:, None, None, None, :]
        scores = jnp.where(pad, NEG_INF, scores)
        causal = jnp.tril(jnp.ones((S, S), bool))[None, :, None, None, :]
        scores = jnp.where(causal, scores, NEG_INF)
        attn = jax.nn.softmax(scores, axis=-1)
        out = jnp.einsum('bnghm,bmgd->bnghd', attn, v).reshape(B, S, D)
        return out @ w_o.T + b_o

    def _L0_ffn_ref(x, Wg, W1, W3, W2, Ws1, Ws3, Ws2):
        import jax, jax.numpy as jnp
        import numpy as np
        DIM = 512
        INTER = 352
        E = 16
        TOPK = 4
        G = 4
        TOPK_G = 2
        N_SHARED = 2
        SHARED_INTER = N_SHARED * INTER
        ROUTE_SCALE = 1.0

        def _moe_forward(x, Wg, W1, W3, W2, Ws1, Ws3, Ws2):
            B, S, D = x.shape
            xt = x.reshape(-1, D)
            T = xt.shape[0]
            scores = jax.nn.softmax(xt @ Wg.T, axis=-1)
            sg = scores.reshape(T, G, E // G)
            group_scores = sg.max(axis=-1)
            gidx = jax.lax.top_k(group_scores, TOPK_G)[1]
            gmask = jax.nn.one_hot(gidx, G, dtype=jnp.float32).sum(axis=1) > 0
            masked = jnp.where(gmask[:, :, None], sg, -jnp.inf).reshape(T, E)
            topi = jax.lax.top_k(masked, TOPK)[1]
            weights = jnp.take_along_axis(scores, topi, axis=1) * ROUTE_SCALE
            combine = jnp.zeros((T, E), xt.dtype).at[jnp.arange(T)[:, None], topi].add(weights)
            h = jax.nn.silu(jnp.einsum('td,eid->eti', xt, W1)) * jnp.einsum('td,eid->eti', xt, W3)
            expert_out = jnp.einsum('eti,edi->etd', h, W2)
            y = jnp.einsum('etd,te->td', expert_out, combine)
            z = jax.nn.silu(xt @ Ws1.T) * (xt @ Ws3.T) @ Ws2.T
            return (y + z).reshape(B, S, D)
        return _moe_forward(x, Wg, W1, W3, W2, Ws1, Ws3, Ws2)
    x = x + jnp.tanh(g_xattn[0]) * _L0_xattn_ref(_layernorm(x, axis=-1), ctx_2048, ctx_2048, mask_BxS2_if1, L0_xattn_w_q, L0_xattn_w_k, L0_xattn_w_v, L0_xattn_w_o, L0_xattn_b_o)
    x = x + jnp.tanh(g_ffn[0]) * _L0_ffn_ref(_layernorm(x, axis=-1), L0_ffn_Wg, L0_ffn_W1, L0_ffn_W3, L0_ffn_W2, L0_ffn_Ws1, L0_ffn_Ws3, L0_ffn_Ws2)
    return x

_drawn_inputs = setup_inputs


def setup_inputs(seed=0):
    import zlib

    import numpy as np

    out = dict(_drawn_inputs(seed))
    spreads = {'L0_xattn_b_o': (0.0, 0.1)}
    factors = {'L0_xattn_w_q': 8.0,
     'L0_xattn_w_k': 8.0,
     'L0_ffn_Wg': 7.919,
     'L0_ffn_W1': 6.895,
     'L0_ffn_W3': 6.825,
     'L0_ffn_W2': 6.799,
     'L0_ffn_Ws1': 8.0,
     'L0_ffn_Ws3': 8.0,
     'L0_ffn_Ws2': 8.0}
    for name, (base, spread) in spreads.items():
        noise = np.random.default_rng([zlib.crc32(name.encode()), seed]).standard_normal(out[name].shape)
        drawn = base * np.exp(spread * noise) if base else spread * noise
        out[name] = jnp.asarray(drawn.astype(out[name].dtype))
    for name, factor in factors.items():
        out[name] = (out[name] * factor).astype(out[name].dtype)
    return out
```

```python
from contextlib import ExitStack

import numpy as np

import concourse.bass as bass
import concourse.mybir as mybir
from concourse.alu_op_type import AluOpType as ALU

F32 = mybir.dt.float32
F32R = mybir.dt.float32r
BF16 = mybir.dt.bfloat16
I32 = mybir.dt.int32
ACT = mybir.ActivationFunctionType
AX = mybir.AxisListType.X

P = 128
BATCH, SEQ, D = 4, 512, 512
T = BATCH * SEQ
KD = D // P
GROUPS, HG, HD = 8, 4, 16
CH = SEQ // P
NIT = BATCH * GROUPS
VW = 2 * HD
KROWS = 96
ROW_MAX, ROW_PAD = 64, 65
NEG = -1.0e30
EPS = 1e-5

E, EG, TOPG, TOPK = 16, 4, 2, 4
INTER = 352
SHARED = 2 * INTER
ICH = [(0, 128), (128, 128), (256, 96)]
SCH = [(0, 128), (128, 128), (256, 128), (384, 128), (512, 128), (640, 64)]
NT = T // P
TILES = T * TOPK // P + E - 1
LOAD = 3 * 16


def wait(eng, sem, value):
    if not isinstance(value, int) or value > 0:
        eng.wait_ge(sem, value + 1)


def landed(eng, sem, value):
    eng.wait_ge(sem, value)


def start(nc, sems):
    with nc.Block(no_gpsimd_drain=True) as block:
        @block.vector
        def _(eng):
            for sem in sems:
                eng.sem_inc(sem, 1)


def wait_next(eng, sem, due, step):
    eng.wait_ge(sem, eng.snap(due))
    eng.reg_add(due, due, step)


def inverse_deviation(eng, variances, root, rstd, work, s_root, s_step, turn):
    links = iter(range(1, 6))

    def link(ins):
        ins.then_inc(s_step, 1)
        wait(eng, s_step, turn * 5 + next(links))

    wait(eng, s_root, turn + 1)
    link(eng.reciprocal(rstd, root))
    link(eng.tensor_tensor(work, rstd, rstd, ALU.mult))
    link(eng.scalar_tensor_tensor(out=work, in0=variances, scalar=EPS, in1=work, op0=ALU.add, op1=ALU.mult))
    link(eng.tensor_scalar(work, work, -0.5, 1.5, ALU.mult, ALU.add))
    link(eng.tensor_tensor(rstd, rstd, work, ALU.mult))


def stage_project(nc, io, dram):
    with ExitStack() as c:
        sb = lambda n, s, d=F32: c.enter_context(nc.sbuf_tensor(n, s, d))
        ps = lambda n, s: c.enter_context(nc.psum_tensor(n, s, F32))
        sems = []
        dsem = lambda n: c.enter_context(nc.semaphore(n))

        def sem(name):
            sems.append(dsem(name))
            return sems[-1]

        wq, wk, wv = sb("wq", [P, KD, D]), sb("wk", [P, KD, P]), sb("wv", [P, KD, P])
        x, ctx = sb("p_x", [P, CH, D]), sb("p_ctx", [P, KD, SEQ])
        xn, xnT = sb("p_xn", [P, CH, D]), sb("p_xnT", [P, KD, SEQ])
        stats, mv, rstd = sb("p_stats", [P, CH, 6]), sb("p_mv", [P, CH, 2]), sb("p_rstd", [P, CH])
        root, work, eps = sb("p_root", [P, CH]), sb("p_work", [P, CH]), sb("p_eps", [P, 1])
        s_root, s_newton, s_eps = sem("p_sroot"), sem("p_snewton"), sem("p_seps")
        parts = sb("p_parts", [P, KD + 1, 2, SEQ], F32R)
        v = sb("p_v", [P, CH, GROUPS, VW])
        ident = io["ident"]
        padi, padb = sb("p_padi", [BATCH, SEQ], I32), sb("p_padb", [BATCH, SEQ], F32R)
        padf = sb("p_padf", [BATCH, SEQ])
        proj = [ps(f"p_proj{i}", [P, SEQ]) for i in range(KD + 1)]
        vps = ps("p_vps", [P, CH, P])
        tps = [ps(f"p_tps{i}", [P, KD, P]) for i in range(2)]
        s_wq, s_wk, s_wv = dsem("p_swq"), dsem("p_swk"), dsem("p_swv")
        s_x, s_ctx, s_ones, s_kept = dsem("p_sx"), dsem("p_sctx"), sem("p_sones"), sem("p_skept")
        s_st, s_mv, s_xn = sem("p_sst"), sem("p_smv"), sem("p_sxn")
        s_tr, s_xT = sem("p_str"), sem("p_sxT")
        s_kmm, s_vmm, s_qmm = sem("p_skmm"), sem("p_svmm"), sem("p_sqmm")
        s_khi, s_klo, s_qhi, s_qlo, s_vcp = (sem(f"p_s{n}") for n in ("khi", "klo", "qhi", "qlo", "vcp"))
        s_qout = dsem("p_sqout")
        s_kout, s_vout = dsem("p_skout"), dsem("p_svout")
        s_pad, s_padb, s_padf, s_pout = dsem("p_spad"), sem("p_spadb"), sem("p_spadf"), dsem("p_spout")
        start(nc, sems)
        block = c.enter_context(nc.Block())

        @block.sync
        def _(eng):
            eng.dma_start(wk[:], io["wkT"].rearrange("(c p) n -> p c n", p=P)).then_inc(s_wk, 16)
            eng.dma_start(wv[:], io["wvT"].rearrange("(c p) n -> p c n", p=P)).then_inc(s_wv, 16)
            eng.dma_start(wq[:], io["wqT"].rearrange("(c p) n -> p c n", p=P)).then_inc(s_wq, 16)
            eng.dma_start(padi[:], io["mask"]).then_inc(s_pad, 16)
            with eng.Fori(0, BATCH) as b:
                wait(eng, s_vmm, b)
                eng.dma_start(ctx[:], io["ctxT"][:, bass.ts(b, SEQ)].rearrange("(c p) n -> p c n", p=P)).then_inc(s_ctx, 16)
                wait(eng, s_xn, b * CH)
                eng.dma_start(x[:], io["x"][bass.ts(b, SEQ), :].rearrange("(j p) d -> p j d", p=P)).then_inc(s_x, 16)
            wait(eng, s_padb, 1)
            for b in range(BATCH):
                for g in range(GROUPS):
                    eng.dma_start(dram["pad"][b * GROUPS + g:b * GROUPS + g + 1, :], padb[b:b + 1, :].bitcast(F32)).then_inc(s_pout, 16)
            landed(eng, s_pout, 16 * NIT)

        @block.gpsimd
        def _(eng):
            eng.memset(v[:], 1.0).then_inc(s_ones, 1)
            eng.memset(eps[:], EPS).then_inc(s_eps, 1)
            with eng.Fori(0, BATCH) as b:
                wait(eng, s_vcp, b + 1)
                for j in range(CH):
                    eng.dma_start(dram["v"][bass.ts(b, GROUPS), j * P:(j + 1) * P].rearrange("g p w -> p g w"), v[:, j]).then_inc(s_vout, 16)
                wait(eng, s_klo, b + 1)
                for g in range(GROUPS):
                    for rep in range(2):
                        eng.dma_start(dram["k"][bass.ds(b * GROUPS + g, 1), :, rep].rearrange("i s d n -> (i d) s n"),
                                      parts[g * HD:(g + 1) * HD, KD].bitcast(F32)).then_inc(s_kout, 16)
                for i in range(KD):
                    wait(eng, s_qlo, b * KD + i + 1)
                    for g in range(2):
                        eng.dma_start(dram["q"][bass.ds(b * GROUPS + 2 * i + g, 1)].rearrange("i s p n -> (i p) s n"),
                                      parts[64 * g:64 * g + 64, i].bitcast(F32)).then_inc(s_qout, 16)
                landed(eng, s_vout, 16 * CH * (b + 1))
                landed(eng, s_kout, 32 * GROUPS * (b + 1))
                landed(eng, s_qout, 32 * KD * (b + 1))
                eng.sem_inc(s_kept, 1)

        @block.vector
        def _(eng):
            due = eng.alloc_register("due0")
            eng.reg_mov(due, CH + 1)
            landed(eng, s_pad, 16)
            eng.tensor_copy(padf[:], padi[:]).then_inc(s_padf, 1)
            wait(eng, s_padf, 1)
            eng.tensor_scalar(padb[:], padf[:], 0.0, NEG, ALU.is_equal, ALU.mult).then_inc(s_padb, 1)
            with eng.Fori(0, BATCH) as b:
                landed(eng, s_x, 16 * (b + 1))
                for j in range(CH):
                    eng.bn_stats(stats[:, j, :], x[:, j, :]).then_inc(s_st, 1)
                wait_next(eng, s_st, due, CH)
                for j in range(CH):
                    eng.bn_aggr(mv[:, j, :], stats[:, j, :]).then_inc(s_mv, 1)
                inverse_deviation(eng, mv[:, :, 1], root[:], rstd[:], work[:], s_root, s_newton, b)
                wait(eng, s_tr, b * CH)
                for j in range(CH):
                    eng.tensor_scalar(xn[:, j, :], x[:, j, :], mv[:, j, 0:1], rstd[:, j:j + 1],
                                      ALU.subtract, ALU.mult).then_inc(s_xn, 1)
                wait(eng, s_khi, b + 1)
                eng.tensor_tensor(parts[:, KD, 1, :], proj[KD][:], parts[:, KD, 0, :].bitcast(F32), ALU.subtract).then_inc(s_klo, 1)
                for i in range(KD):
                    wait(eng, s_qhi, b * KD + i + 1)
                    eng.tensor_tensor(parts[:, i, 1, :], proj[i][:], parts[:, i, 0, :].bitcast(F32), ALU.subtract).then_inc(s_qlo, 1)

        @block.scalar
        def _(eng):
            wait(eng, s_ones, 1)
            wait(eng, s_eps, 1)
            with eng.Fori(0, BATCH) as b:
                wait(eng, s_kmm, b + 1)
                wait(eng, s_kept, b)
                eng.activation(parts[:, KD, 0, :], proj[KD][:], ACT.Copy).then_inc(s_khi, 1)
                wait(eng, s_vmm, b + 1)
                eng.activation(v[:, :, :, 0:HD], vps[:].rearrange("p j (g w) -> p j g w", g=GROUPS), ACT.Copy).then_inc(s_vcp, 1)
                wait(eng, s_mv, (b + 1) * CH)
                eng.activation(root[:], mv[:, :, 1], ACT.Sqrt, bias=eps[:]).then_inc(s_root, 1)
                for j in range(CH):
                    wait(eng, s_tr, b * CH + j + 1)
                    eng.activation(xnT[:, :, j * P:(j + 1) * P], tps[j % 2][:], ACT.Copy).then_inc(s_xT, 1)
                for i in range(KD):
                    wait(eng, s_qmm, b * KD + i + 1)
                    eng.activation(parts[:, i, 0, :], proj[i][:], ACT.Copy).then_inc(s_qhi, 1)

        @block.tensor
        def _(eng):
            for s in (s_wk, s_wv, s_wq):
                landed(eng, s, 16)
            with eng.Fori(0, BATCH) as b:
                landed(eng, s_ctx, 16 * (b + 1))
                wait(eng, s_klo, b)
                for k in range(KD):
                    mm = eng.matmul(proj[KD][:], wk[:, k, :], ctx[:, k, :], start=k == 0, stop=k == KD - 1)
                mm.then_inc(s_kmm, 1)
                wait(eng, s_vcp, b)
                for j in range(CH):
                    for k in range(KD):
                        mm = eng.matmul(vps[:, j, :], ctx[:, k, j * P:(j + 1) * P], wv[:, k, :], start=k == 0, stop=k == KD - 1)
                mm.then_inc(s_vmm, 1)
                for j in range(CH):
                    wait(eng, s_xn, b * CH + j + 1)
                    if j >= 2:
                        wait(eng, s_xT, b * CH + j - 1)
                    else:
                        wait(eng, s_xT, b * CH)
                    for k in range(KD):
                        mm = eng.transpose(tps[j % 2][:, k, :], xn[:, j, k * P:(k + 1) * P], ident)
                    mm.then_inc(s_tr, 1)
                wait(eng, s_xT, (b + 1) * CH)
                wait(eng, s_qlo, b * KD)
                for i in range(KD):
                    for k in range(KD):
                        mm = eng.matmul(proj[i][:], wq[:, k, i * P:(i + 1) * P], xnT[:, k, :], start=k == 0, stop=k == KD - 1)
                    mm.then_inc(s_qmm, 1)


def stage_constants(nc, io):
    with ExitStack() as c:
        sems = s_m, s_c = c.enter_context(nc.semaphore("c_sm")), c.enter_context(nc.semaphore("c_sc"))
        start(nc, sems)
        block = c.enter_context(nc.Block())

        @block.gpsimd
        def _(eng):
            eng.memset(io["ident"], 0.0).then_inc(s_m, 1)
            eng.memset(io["identb"], 0.0).then_inc(s_m, 1)
            eng.memset(io["late_col"], 0.0).then_inc(s_m, 1)
            eng.memset(io["late_row"], 0.0).then_inc(s_m, 1)
            eng.memset(io["before"], 1.0).then_inc(s_m, 1)
            eng.memset(io["onesb"], 1.0).then_inc(s_m, 1)
            wait(eng, s_m, 6)

            def sel(t, op, fill, sign=1):
                eng.affine_select(out=t, in_=t, compare_op=op, fill=fill, base=0, pattern=[[-sign, P]],
                                  channel_multiplier=sign).then_inc(s_c, 1)
            sel(io["ident"], ALU.not_equal, 1.0)
            sel(io["identb"], ALU.not_equal, 1.0)
            sel(io["late_col"], ALU.is_ge, NEG)
            sel(io["late_row"], ALU.is_ge, NEG, -1)
            sel(io["before"], ALU.is_gt, 0.0, -1)
            wait(eng, s_c, 5)


def stage_attend(nc, io, dram):
    NB, AHEAD = 4, 2
    with ExitStack() as c:
        sb = lambda n, s, d=F32: c.enter_context(nc.sbuf_tensor(n, s, d))
        ps = lambda n, s: c.enter_context(nc.psum_tensor(n, s, F32))
        sems = []
        dsem = lambda n: c.enter_context(nc.semaphore(n))

        def sem(name):
            sems.append(dsem(name))
            return sems[-1]

        q = [sb(f"a_q{i}", [KROWS, HG, SEQ], F32R) for i in range(NB)]
        k = [sb(f"a_k{i}", [KROWS, SEQ], F32R) for i in range(NB)]
        v = [sb(f"a_v{i}", [P, CH, VW]) for i in range(NB)]
        const = sb("a_const", [1, 2, HG * SEQ])
        at = [sb(f"a_at{i}", [P, CH, HG, SEQ]) for i in range(2)]
        mx, negm = sb("a_mx", [P, HG, CH]), sb("a_negm", [P, HG, CH])
        mrow = [sb(f"a_mrow{i}", [HG * CH, P], F32R) for i in range(2)]
        o = sb("a_o", [P, SEQ])
        mb = [ps(f"a_mb{i}", [P, SEQ]) for i in range(2)]
        eb = [ps(f"a_eb{i}", [P, 2, SEQ]) for i in range(2)]
        pv, mt = ps("a_pv", [P, SEQ]), ps("a_mt", [HG * CH, P])
        s_init, s_one, s_out = sem("a_sinit"), dsem("a_sone"), dsem("a_sout")
        s_ld = [dsem(f"a_sld{i}") for i in range(NB)]
        s_smax, s_rmax, s_negm, s_mt, s_mr = (sem(f"a_s{n}") for n in ("smax", "rmax", "negm", "mt", "mr"))
        s_row = [dsem(f"a_srow{i}") for i in range(NB)]
        s_sexp, s_exp, s_pv, s_o, s_kept = (sem(f"a_s{n}") for n in ("sexp", "exp", "pv", "o", "kept"))
        LD = 6 * 16
        start(nc, sems)
        block = c.enter_context(nc.Block())

        def steps(eng, body):
            with eng.Fori(0, NIT // NB - 1) as t:
                for r in range(NB):
                    body(t * NB + r, r, t)
            for r in range(NB):
                body(NIT - NB + r, r, NIT // NB - 1)

        def exists(i):
            return not isinstance(i, int) or i < NIT

        @block.gpsimd
        def _(eng):
            for z in range(2):
                eng.memset(const[:, z, :], float(z)).then_inc(s_init, 1)
            for r in range(NB):
                eng.memset(q[r][64:KROWS].bitcast(F32), 0.0).then_inc(s_init, 1)
                eng.memset(k[r][64:KROWS].bitcast(F32), 0.0).then_inc(s_init, 1)
            wait(eng, s_init, 2 + 2 * NB)
            for r in range(NB):
                eng.memset(k[r][ROW_MAX:ROW_MAX + 1].bitcast(F32), 1.0).then_inc(s_init, 1)
                eng.dma_start(q[r][ROW_PAD:ROW_PAD + 1].bitcast(F32).rearrange("p h n -> p (h n)"), const[:, 1, :]).then_inc(s_one, 16)
            landed(eng, s_one, 16 * NB)

            def body(i, r, t):
                wait(eng, s_o, i + 1)
                eng.dma_start(dram["o"][bass.ds(i, 1)].rearrange("i p n -> (i p) n"), o[:]).then_inc(s_out, 16)
                landed(eng, s_out, 16 * (i + 1))
                eng.sem_inc(s_kept, 1)
            steps(eng, body)

        @block.sync
        def _(eng):
            wait(eng, s_init, 2 + 3 * NB)

            def load(i, r):
                eng.dma_start(q[r][0:32].bitcast(F32).rearrange("p h n -> p (h n)"), dram["q"][bass.ds(i, 1)].rearrange("i s (d h) n -> (i s d) (h n)", h=HG)).then_inc(s_ld[r], 16)
                eng.dma_start(q[r][32:64].bitcast(F32).rearrange("p h n -> p (h n)"), dram["q"][bass.ds(i, 1)].rearrange("i s (d h) n -> (i s d) (h n)", h=HG)).then_inc(s_ld[r], 16)
                eng.dma_start(q[r][ROW_MAX:ROW_MAX + 1].bitcast(F32).rearrange("p h n -> p (h n)"), const[:, 0, :]).then_inc(s_ld[r], 16)
                eng.dma_start(k[r][0:64].bitcast(F32), dram["k"][bass.ds(i, 1)].rearrange("i s r d n -> (i s r d) n")).then_inc(s_ld[r], 16)
                eng.dma_start(k[r][ROW_PAD:ROW_PAD + 1].bitcast(F32), dram["pad"][bass.ds(i, 1), :]).then_inc(s_ld[r], 16)
                eng.dma_start(v[r][:], dram["v"][bass.ds(i, 1)].rearrange("i (c p) w -> p (i c) w", p=P)).then_inc(s_ld[r], 16)

            def body(i, r, t):
                if exists(i + AHEAD + 1):
                    wait(eng, s_pv, i)
                    load(i + AHEAD + 1, (r + AHEAD + 1) % NB)
                if exists(i + AHEAD):
                    wait(eng, s_mr, i + AHEAD + 1)
                    put_row(i + AHEAD, (r + AHEAD) % NB)

            def put_row(i, r):
                eng.dma_start(q[r][ROW_MAX:ROW_MAX + 1].bitcast(F32), mrow[r % 2][:].bitcast(F32)).then_inc(s_row[r], 16)

            for i in range(AHEAD + 1):
                load(i, i)
            for i in range(AHEAD):
                wait(eng, s_mr, i + 1)
                put_row(i, i)
            steps(eng, body)

        @block.scalar
        def _(eng):
            def body(i, r, t):
                for ch in range(CH):
                    for hp in range(2):
                        e = i * 2 * CH + 2 * ch + hp
                        wait(eng, s_sexp, e + 1)
                        eng.activation(at[r % 2][:, ch, 2 * hp:2 * hp + 2, ch * P:SEQ], eb[hp][:, :, ch * P:SEQ],
                                       ACT.Exp, scale=0.25).then_inc(s_exp, 1)
            steps(eng, body)

        @block.vector
        def _(eng):
            def maxima(i, r):
                for ch in range(CH):
                    for h in range(HG):
                        u = i * CH * HG + ch * HG + h
                        wait(eng, s_smax, u + 1)
                        eng.tensor_reduce(mx[:, h, ch:ch + 1], mb[h % 2][:, 0:(ch + 1) * P], AX, ALU.max).then_inc(s_rmax, 1)
                wait(eng, s_rmax, (i + 1) * CH * HG)
                wait(eng, s_mt, i)
                eng.tensor_scalar(negm[:], mx[:], -1.0, None, ALU.mult).then_inc(s_negm, 1)

            def rows(i, r):
                wait(eng, s_mt, i + 1)
                eng.tensor_copy(mrow[r % 2][:], mt[:]).then_inc(s_mr, 1)

            for i in range(AHEAD):
                maxima(i, i)
                rows(i, i)

            def body(i, r, t):
                if exists(i + AHEAD):
                    maxima(i + AHEAD, (r + AHEAD) % NB)
                    landed(eng, s_row[r], 16 * (t + 1))
                    rows(i + AHEAD, (r + AHEAD) % NB)
                wait(eng, s_pv, i + 1)
                wait(eng, s_kept, i)
                eng.tensor_copy(o[:], pv[:]).then_inc(s_o, 1)
            steps(eng, body)

        @block.tensor
        def _(eng):
            def max_units(i, r, t, ch):
                w = max(256, (ch + 1) * P)
                for h in range(HG):
                    u = i * CH * HG + ch * HG + h
                    if not isinstance(i, int) or i * CH * HG + ch * HG + h >= 2:
                        wait(eng, s_rmax, u - 1)
                    if ch == 0 and h == 0:
                        landed(eng, s_ld[r], LD * (t + 1))
                    eng.matmul(mb[h % 2][:, 0:w], q[r][:, h, ch * P:(ch + 1) * P], k[r][:, 0:w], start=True, stop=True)
                    eng.matmul(mb[h % 2][:, ch * P:(ch + 1) * P], io["identb"], io["late_col"], start=False, stop=True,
                               skip_group_check=True).then_inc(s_smax, 1)

            def turn_maxima(i):
                wait(eng, s_negm, i + 1)
                if not isinstance(i, int) or i >= 1:
                    wait(eng, s_mr, i)
                eng.transpose(mt[:], negm[:].rearrange("p h c -> p (h c)"), io["ident"]).then_inc(s_mt, 1)

            def exp_units(i, r, ch):
                n0 = min(ch * P, 256)
                for hp in range(2):
                    if ch:
                        wait(eng, s_exp, i * 2 * CH + 2 * ch + hp - 1)
                    for h in range(2):
                        eng.matmul(eb[hp][:, h, n0:SEQ], k[r][:, ch * P:(ch + 1) * P], q[r][:, 2 * hp + h, n0:SEQ], start=True, stop=True)
                        mm = eng.matmul(eb[hp][:, h, ch * P:(ch + 1) * P], io["identb"], io["late_row"], start=False, stop=True,
                                        skip_group_check=True)
                    mm.then_inc(s_sexp, 1)

            def pv_units(i, r, ch):
                wait(eng, s_exp, i * 2 * CH + 2 * ch + 2)
                if ch == 0:
                    wait(eng, s_o, i)
                for h in range(HG):
                    mm = eng.matmul(pv[32 * h:32 * h + 32, ch * P:SEQ], v[r][:, ch, :], at[r % 2][:, ch, h, ch * P:SEQ],
                                    start=ch == 0, stop=ch == CH - 1, skip_group_check=True, tile_position=(0, 32 * h))
                if ch == CH - 1:
                    mm.then_inc(s_pv, 1)

            wait(eng, s_init, 2 + 3 * NB)
            landed(eng, s_one, 16 * NB)
            for i in range(AHEAD):
                for ch in range(CH):
                    max_units(i, i, 0, ch)
                turn_maxima(i)

            def body(i, r, t):
                landed(eng, s_row[r], 16 * (t + 1))
                for ch in range(CH):
                    exp_units(i, r, ch)
                    if exists(i + AHEAD):
                        max_units(i + AHEAD, (r + AHEAD) % NB, t + (r + AHEAD) // NB, ch)
                    if ch:
                        pv_units(i, r, ch - 1)
                if exists(i + AHEAD):
                    turn_maxima(i + AHEAD)
                pv_units(i, r, CH - 1)
            steps(eng, body)


def stage_close(nc, io, dram):
    with ExitStack() as c:
        sb = lambda n, s, d=F32: c.enter_context(nc.sbuf_tensor(n, s, d))
        ps = lambda n, s: c.enter_context(nc.psum_tensor(n, s, F32))
        sems = []
        dsem = lambda n: c.enter_context(nc.semaphore(n))

        def sem(name):
            sems.append(dsem(name))
            return sems[-1]

        wo, wg = sb("c_wo", [P, KD, D]), sb("c_wg", [P, KD, E])
        bo, gx, tg = sb("c_bo", [P, D]), sb("c_gx", [P, 1]), sb("c_tg", [P, 1])
        o, den, x = sb("c_o", [P, KD, SEQ]), sb("c_den", [P, KD, SEQ]), sb("c_x", [P, CH, D])
        y, x1, x2 = sb("c_y", [P, CH, D]), sb("c_x1", [P, CH, D]), sb("c_x2", [P, CH, D])
        x2T = sb("c_x2T", [P, KD, SEQ])
        stats, mv, rstd = sb("c_stats", [P, CH, 6]), sb("c_mv", [P, CH, 2]), sb("c_rstd", [P, CH])
        root, work, eps = sb("c_root", [P, CH]), sb("c_work", [P, CH]), sb("c_eps", [P, 1])
        s_root, s_newton, s_eps = sem("c_sroot"), sem("c_snewton"), sem("c_seps")
        op = [ps(f"c_op{i}", [P, D]) for i in range(CH)]
        tp = [ps(f"c_tp{i}", [P, KD, P]) for i in range(2)]
        lp = ps("c_lp", [P, CH, E])
        s_w, s_g, s_o, s_x = (dsem(f"c_s{n}") for n in ("w", "g", "o", "x"))
        s_tg, s_kept = sem("c_stg"), sem("c_skept")
        s_rec, s_on, s_op, s_y, s_x1, s_st, s_mv, s_x2 = (
            sem(f"c_s{n}") for n in ("rec", "on", "op", "y", "x1", "st", "mv", "x2"))
        s_tr, s_xT, s_lg, s_lc = (sem(f"c_s{n}") for n in ("tr", "xT", "lg", "lc"))
        s_out = dsem("c_sout")
        LDO = 2 * 8 * 16
        start(nc, sems)
        block = c.enter_context(nc.Block())

        @block.sync
        def _(eng):
            eng.dma_start(wo[:], io["woT"].rearrange("(c p) n -> p c n", p=P)).then_inc(s_w, 16)
            eng.dma_start(wg[:], io["wgT"].rearrange("(c p) n -> p c n", p=P)).then_inc(s_w, 16)
            eng.dma_start(bo[:], io["bo"].broadcast_to([P, D])).then_inc(s_w, 16)
            eng.dma_start(gx[:], io["gx"].broadcast_to([P, 1])).then_inc(s_g, 16)
            with eng.Fori(0, BATCH) as b:
                wait(eng, s_op, b * CH)
                for g2 in range(2):
                    for h in range(HG):
                        for part, t in ((0, o), (1, den)):
                            src = dram["o"][bass.ts(b, GROUPS)].rearrange("(c g) p n -> g p c n", g=2)
                            r0 = 32 * h + HD * part
                            eng.dma_start(t[64 * g2 + HD * h:64 * g2 + HD * h + HD], src[g2, r0:r0 + HD]).then_inc(s_o, 16)
                wait(eng, s_x1, b * CH)
                eng.dma_start(x[:], io["x"][bass.ts(b, SEQ), :].rearrange("(j p) d -> p j d", p=P)).then_inc(s_x, 16)

        @block.gpsimd
        def _(eng):
            due = eng.alloc_register("due1")
            eng.reg_mov(due, CH + 1)
            eng.memset(eps[:], EPS).then_inc(s_eps, 1)
            with eng.Fori(0, BATCH) as b:
                wait(eng, s_x1, (b + 1) * CH)
                eng.dma_start(dram["x1"][bass.ts(b, SEQ), :].rearrange("(j p) d -> p j d", p=P), x1[:]).then_inc(s_out, 16)
                wait_next(eng, s_x2, due, CH)
                eng.dma_start(dram["x2"][bass.ts(b, SEQ), :].rearrange("(j p) d -> p j d", p=P), x2[:]).then_inc(s_out, 16)
                wait(eng, s_xT, (b + 1) * CH)
                eng.dma_start(dram["xT"][bass.ds(b, 1)].rearrange("b p k n -> p (b k) n"), x2T[:]).then_inc(s_out, 16)
                landed(eng, s_out, 48 * (b + 1))
                eng.sem_inc(s_kept, 1)

        @block.scalar
        def _(eng):
            landed(eng, s_g, 16)
            eng.activation(tg[:], gx[:], ACT.Tanh).then_inc(s_tg, 1)
            wait(eng, s_eps, 1)
            with eng.Fori(0, BATCH) as b:
                wait(eng, s_mv, (b + 1) * CH)
                eng.activation(root[:], mv[:, :, 1], ACT.Sqrt, bias=eps[:]).then_inc(s_root, 1)
                wait(eng, s_kept, b)
                wait(eng, s_lg, b)
                for j in range(CH):
                    wait(eng, s_tr, b * CH + j + 1)
                    eng.activation(x2T[:, :, j * P:(j + 1) * P], tp[j % 2][:], ACT.Copy).then_inc(s_xT, 1)

        @block.vector
        def _(eng):
            due = eng.alloc_register("due2")
            eng.reg_mov(due, CH + 1)
            landed(eng, s_w, 48)
            wait(eng, s_tg, 1)
            with eng.Fori(0, BATCH) as b:
                landed(eng, s_o, LDO * (b + 1))
                eng.reciprocal(den[:], den[:]).then_inc(s_rec, 1)
                wait(eng, s_rec, b + 1)
                eng.tensor_tensor(o[:], o[:], den[:], ALU.mult).then_inc(s_on, 1)
                for j in range(CH):
                    wait(eng, s_op, b * CH + j + 1)
                    eng.tensor_tensor(y[:, j, :], op[j][:], bo[:], ALU.add).then_inc(s_y, 1)
                landed(eng, s_x, 16 * (b + 1))
                wait(eng, s_kept, b)
                for j in range(CH):
                    wait(eng, s_y, b * CH + j + 1)
                    eng.scalar_tensor_tensor(out=x1[:, j, :], in0=y[:, j, :], scalar=tg[:, 0:1], in1=x[:, j, :],
                                             op0=ALU.mult, op1=ALU.add).then_inc(s_x1, 1)
                for j in range(CH):
                    wait(eng, s_x1, b * CH + j + 1)
                    eng.bn_stats(stats[:, j, :], x1[:, j, :]).then_inc(s_st, 1)
                wait_next(eng, s_st, due, CH)
                for j in range(CH):
                    eng.bn_aggr(mv[:, j, :], stats[:, j, :]).then_inc(s_mv, 1)
                inverse_deviation(eng, mv[:, :, 1], root[:], rstd[:], work[:], s_root, s_newton, b)
                for j in range(CH):
                    eng.tensor_scalar(x2[:, j, :], x1[:, j, :], mv[:, j, 0:1], rstd[:, j:j + 1],
                                      ALU.subtract, ALU.mult).then_inc(s_x2, 1)
                wait(eng, s_lg, b + 1)
                eng.tensor_copy(io["logits"][:, bass.ts(b, CH), :], lp[:]).then_inc(s_lc, 1)

        @block.tensor
        def _(eng):
            landed(eng, s_w, 48)
            with eng.Fori(0, BATCH) as b:
                wait(eng, s_on, b + 1)
                for j in range(CH):
                    for k in range(KD):
                        mm = eng.matmul(op[j][:], o[:, k, j * P:(j + 1) * P], wo[:, k, :], start=k == 0, stop=k == KD - 1)
                    mm.then_inc(s_op, 1)
                for j in range(CH):
                    wait(eng, s_x2, b * CH + j + 1)
                    wait(eng, s_xT, b * CH + max(0, j - 1))
                    for k in range(KD):
                        mm = eng.transpose(tp[j % 2][:, k, :], x2[:, j, k * P:(k + 1) * P], io["ident"])
                    mm.then_inc(s_tr, 1)
                wait(eng, s_xT, (b + 1) * CH)
                wait(eng, s_lc, b)
                for j in range(CH):
                    for k in range(KD):
                        mm = eng.matmul(lp[:, j, :], x2T[:, k, j * P:(j + 1) * P], wg[:, k, :], start=k == 0, stop=k == KD - 1)
                mm.then_inc(s_lg, 1)


def stage_route(nc, io, dram):
    with ExitStack() as c:
        sb = lambda n, s, d=F32: c.enter_context(nc.sbuf_tensor(n, s, d))
        sems = []
        dsem = lambda n: c.enter_context(nc.semaphore(n))

        def sem(name):
            sems.append(dsem(name))
            return sems[-1]

        NG, NK = E // EG, TOPK
        big = lambda n, d=F32: sb(n, [P, NT, E], d)
        z, score, masked, slot, sel, prod = (big(f"r_{n}") for n in ("z", "score", "masked", "slot", "sel", "prod"))
        chosen = big("r_chosen", BF16)
        one = [sb(f"r_one{k}", [P, NT, E]) for k in range(NK)]
        top, topi, topf = sb("r_top", [P, NT, 8]), sb("r_topi", [P, NT, 8], mybir.dt.uint32), sb("r_topf", [P, NT, 8])
        mx, den = sb("r_mx", [P, NT, 1]), sb("r_den", [P, NT, 1])
        gm, grank, gtmp = sb("r_gm", [P, NT, NG]), sb("r_grank", [P, NT, NG]), sb("r_gtmp", [P, NT, NG])
        tot, before = sb("r_tot", [P, NT, E]), sb("r_before", [P, NT, E])
        count, counti = sb("r_count", [P, E]), sb("r_counti", [P, E], I32)
        tiles, base, base0, onesE = (sb(f"r_{n}", [P, E]) for n in ("tiles", "base", "base0", "onesE"))
        slotf = sb("r_slotf", [P, NT, NK])
        iota_e, iota_g = sb("r_iotae", [P, E]), sb("r_iotag", [1, TILES])
        iota_i, tok_i, iotag_i = sb("r_iotai", [P, E], I32), sb("r_toki", [P, NT], I32), sb("r_iotagi", [1, TILES], I32)
        tok, zero = sb("r_tok", [P, NT]), sb("r_zero", [TILES, P])
        cmp, tile_e, tile_b = sb("r_cmp", [1, TILES, E]), sb("r_tilee", [1, TILES]), sb("r_tileb", [1, TILES])
        turned = sb("r_turned", [TILES, P])
        within = c.enter_context(nc.psum_tensor("r_within", [P, NT, E], F32))
        totals = c.enter_context(nc.psum_tensor("r_totals", [P, NT, E], F32))
        tokps = c.enter_context(nc.psum_tensor("r_tokps", [P, TILES], F32))
        s_c, s_i, s_exp, s_ch, s_mm, s_slot, s_zero, s_t, s_v = (
            sem(f"r_s{n}") for n in ("c", "i", "exp", "ch", "mm", "slot", "zero", "t", "v"))
        s_put, s_back = dsem("r_sput"), dsem("r_sback")
        slots = dram["slots"]
        start(nc, sems)
        block = c.enter_context(nc.Block())
        rows = lambda t, n: t.broadcast_to([P, NT, n])

        @block.vector
        def _(eng):
            n = [0]

            def link(ins):
                n[0] += 1
                ins.then_inc(s_v, 1)
                wait(eng, s_v, n[0])

            wait(eng, s_i, 3)
            link(eng.tensor_copy(iota_e[:], iota_i[:]))
            link(eng.tensor_copy(tok[:], tok_i[:]))
            link(eng.tensor_copy(iota_g[:], iotag_i[:]))
            link(eng.memset(onesE[:], 1.0))
            link(eng.tensor_reduce(mx[:], io["logits"], AX, ALU.max))
            eng.tensor_tensor(z[:], io["logits"], rows(mx[:], E), ALU.subtract).then_inc(s_c, 1)
            wait(eng, s_exp, 1)
            link(eng.tensor_reduce(den[:], z[:], AX, ALU.add))
            link(eng.reciprocal(den[:], den[:]))
            link(eng.tensor_tensor(score[:], z[:], rows(den[:], E), ALU.mult))
            link(eng.tensor_reduce(gm[:], score[:].rearrange("p t (g e) -> p t g e", g=NG), AX, ALU.max))
            link(eng.memset(grank[:], 0.0))
            for j in range(NG):
                lead = gm[:, :, j:j + 1]
                link(eng.memset(gtmp[:], 0.0))
                if j + 1 < NG:
                    link(eng.tensor_tensor(gtmp[:, :, j + 1:NG], rows(lead, NG - j - 1), gm[:, :, j + 1:NG], ALU.is_ge))
                if j:
                    link(eng.tensor_tensor(gtmp[:, :, 0:j], rows(lead, j), gm[:, :, 0:j], ALU.is_gt))
                link(eng.tensor_tensor(grank[:], grank[:], gtmp[:], ALU.add))
            link(eng.tensor_scalar(grank[:], grank[:], float(TOPG), None, ALU.is_lt))
            link(eng.tensor_scalar(gtmp[:], grank[:], 1.0, None, ALU.subtract))
            for g in range(NG):
                part = slice(g * EG, (g + 1) * EG)
                link(eng.tensor_tensor(masked[:, :, part], score[:, :, part], rows(grank[:, :, g:g + 1], EG), ALU.mult))
                link(eng.tensor_tensor(masked[:, :, part], masked[:, :, part], rows(gtmp[:, :, g:g + 1], EG), ALU.add))
            for t in range(NT):
                link(eng.max(top[:, t, :], masked[:, t, :]))
                link(eng.max_index(topi[:, t, :], top[:, t, :], masked[:, t, :]))
            link(eng.tensor_copy(topf[:], topi[:]))
            link(eng.tensor_copy(io["weight"], top[:, :, 0:NK]))
            for k in range(NK):
                link(eng.tensor_tensor(one[k][:], iota_e[:].rearrange("p (o e) -> p o e", o=1).broadcast_to([P, NT, E]),
                                       rows(topf[:, :, k:k + 1], E), ALU.is_equal))
            link(eng.tensor_tensor(sel[:], one[0][:], one[1][:], ALU.add))
            link(eng.tensor_tensor(sel[:], sel[:], one[2][:], ALU.add))
            eng.tensor_tensor(chosen[:], sel[:], one[3][:], ALU.add).then_inc(s_ch, 1)
            wait(eng, s_mm, 2)
            link(eng.tensor_copy(tot[:], totals[:]))
            link(eng.memset(before[:, 0, :], 0.0))
            for t in range(1, NT):
                link(eng.tensor_tensor(before[:, t, :], before[:, t - 1, :], tot[:, t - 1, :], ALU.add))
            link(eng.tensor_tensor(count[:], before[:, NT - 1, :], tot[:, NT - 1, :], ALU.add))
            link(eng.tensor_scalar(count[:], count[:], float(P - 1), None, ALU.add))
            link(eng.tensor_copy(counti[:], count[:]))
            link(eng.tensor_scalar(counti[:], counti[:], 7, None, ALU.logical_shift_right))
            link(eng.tensor_copy(tiles[:], counti[:]))
            link(eng.tensor_scalar(tiles[:], tiles[:], 1.0, None, ALU.max))
            link(eng.tensor_tensor_scan(base[:], onesE[:], tiles[:], 0.0, ALU.mult, ALU.add))
            link(eng.tensor_tensor(base[:], base[:], tiles[:], ALU.subtract))
            link(eng.tensor_scalar(base0[:], base[:], float(P), None, ALU.mult))
            link(eng.tensor_tensor(slot[:], within[:], before[:], ALU.add))
            link(eng.tensor_tensor(slot[:], slot[:], base0[:].rearrange("p (o e) -> p o e", o=1).broadcast_to([P, NT, E]), ALU.add))
            for k in range(NK):
                link(eng.tensor_tensor(prod[:], slot[:], one[k][:], ALU.mult))
                link(eng.tensor_reduce(slotf[:, :, k:k + 1], prod[:], AX, ALU.add))
            eng.tensor_copy(io["slot"], slotf[:]).then_inc(s_slot, 1)
            link(eng.tensor_tensor(cmp[:], iota_g[:].rearrange("p (g o) -> p g o", o=1).broadcast_to([1, TILES, E]),
                                   base[0:1, :].rearrange("p (o e) -> p o e", o=1).broadcast_to([1, TILES, E]), ALU.is_ge))
            link(eng.tensor_reduce(tile_e[:].rearrange("p (g o) -> p g o", o=1), cmp[:], AX, ALU.add))
            link(eng.tensor_scalar(tile_b[:], tile_e[:], float(LOAD), None, ALU.mult))
            link(eng.tensor_copy(io["landed"], tile_b[:]))
            link(eng.tensor_scalar(tile_e[:], tile_e[:], 1.0, None, ALU.subtract))
            link(eng.tensor_copy(io["expert"], tile_e[:]))
            link(eng.tensor_scalar(io["buffer"], io["expert"], 1, None, ALU.bitwise_and))
            link(eng.tensor_scalar(io["first"][:, 0:E], base[0:1, :], 1.0, None, ALU.add))
            wait(eng, s_t, 1)
            link(eng.tensor_copy(io["token"], tokps[:]))

        @block.scalar
        def _(eng):
            wait(eng, s_c, 1)
            eng.activation(z[:], z[:], ACT.Exp).then_inc(s_exp, 1)

        @block.tensor
        def _(eng):
            wait(eng, s_ch, 1)
            flat = lambda t: t[:].rearrange("p t e -> p (t e)")
            eng.matmul(flat(within), io["before"], flat(chosen), start=True, stop=True).then_inc(s_mm, 1)
            eng.matmul(flat(totals), io["onesb"], flat(chosen), start=True, stop=True).then_inc(s_mm, 1)
            landed(eng, s_back, 16)
            eng.transpose(tokps[:], turned[:], io["ident"][0:TILES, 0:TILES]).then_inc(s_t, 1)

        @block.gpsimd
        def _(eng):
            eng.iota(iota_i[:], pattern=[[1, E]], base=0, channel_multiplier=0).then_inc(s_i, 1)
            eng.iota(tok_i[:], pattern=[[P, NT]], base=0, channel_multiplier=1).then_inc(s_i, 1)
            eng.iota(iotag_i[:], pattern=[[1, TILES]], base=0, channel_multiplier=0).then_inc(s_i, 1)
            eng.memset(zero[:], 0.0).then_inc(s_zero, 1)
            wait(eng, s_zero, 1)
            eng.dma_start(slots.rearrange("(g p) o -> g (p o)", p=P), zero[:]).then_inc(s_put, 16)
            landed(eng, s_put, 16)
            wait(eng, s_slot, 1)
            for t in range(NT):
                for k in range(NK):
                    eng.indirect_dma_start(out=slots, out_offset=bass.IndirectOffsetOnAxis(ap=io["slot"][:, t, k:k + 1], axis=0),
                                           in_=tok[:, t:t + 1], in_offset=None).then_inc(s_put, 16)
            landed(eng, s_put, 16 * (NT * NK + 1))
            eng.dma_start(turned[:], slots.rearrange("(g p) o -> g (p o)", p=P)).then_inc(s_back, 16)
            landed(eng, s_back, 16)


def stage_experts(nc, io, dram):
    NI = len(ICH)
    with ExitStack() as c:
        sb = lambda n, s, d=F32: c.enter_context(nc.sbuf_tensor(n, s, d))
        ps = lambda n, s: c.enter_context(nc.psum_tensor(n, s, F32))
        sems = []
        dsem = lambda n: c.enter_context(nc.semaphore(n))

        def sem(name):
            sems.append(dsem(name))
            return sems[-1]

        w13, w2 = sb("e_w13", [P, 2, KD, 2 * INTER]), sb("e_w2", [P, 2, NI, D])
        idx = [sb(f"e_idx{i}", [P, 1], I32) for i in range(2)]
        x = [sb(f"e_x{i}", [P, D]) for i in range(2)]
        xT = [sb(f"e_xT{i}", [P, KD, P]) for i in range(2)]
        act = [sb(f"e_act{i}", [P, INTER]) for i in range(2)]
        h = [sb(f"e_h{i}", [P, INTER]) for i in range(2)]
        hT = [sb(f"e_hT{i}", [P, NI, P]) for i in range(2)]
        y = sb("e_y", [P, D])
        xps, hps, yps = ps("e_xps", [P, KD, P]), ps("e_hps", [P, NI, P]), ps("e_yps", [P, D])
        gate = [ps(f"e_gate{i}", [P, INTER]) for i in range(2)]
        up = [ps(f"e_up{i}", [P, INTER]) for i in range(2)]
        s_idx = sem("e_sidx")
        s_x = [dsem(f"e_sx{i}") for i in range(2)]
        s_w, s_out = dsem("e_sw"), dsem("e_sout")
        s_kept, s_xt, s_xT, s_gate, s_up, s_act, s_h, s_ht, s_hT, s_down, s_y = (
            sem(f"e_s{n}") for n in ("kept", "xt", "xT", "gate", "up", "act", "h", "ht", "hT", "down", "y"))
        start(nc, sems)
        block = c.enter_context(nc.Block())
        LAST = TILES - 1

        def tiles(eng, body):
            body(0, 0)
            with eng.Fori(0, (LAST - 2) // 2) as t:
                body(t * 2 + 1, 1, t)
                body(t * 2 + 2, 0, t + 1)
            body(LAST - 1, (LAST - 1) % 2)
            body(LAST, LAST % 2)

        def exists(g):
            return not isinstance(g, int) or 0 <= g <= LAST

        @block.sync
        def _(eng):
            def load(e, buf):
                eng.dma_start(w13[:, buf], io["w13T"][bass.ds(e, 1)].rearrange("e (c p) n -> p (e c) n", p=P)).then_inc(s_w, 16)
                eng.dma_start(w2[:, buf, 0:2], io["w2T"][bass.ds(e, 1), 0:2 * P].rearrange("e (c p) n -> p (e c) n", p=P)).then_inc(s_w, 16)
                eng.dma_start(w2[0:INTER - 2 * P, buf, 2], io["w2T"][bass.ds(e, 1), 2 * P:INTER].rearrange("e p n -> (e p) n")).then_inc(s_w, 16)

            for e in range(2):
                load(e, e)
                landed(eng, s_w, LOAD * (e + 1))
            with eng.Fori(1, E // 2) as u:
                for r in range(2):
                    free = eng.value_load(io["first"][0:1, bass.ds(u * 2 + r - 1, 1)], min_val=0, max_val=TILES)
                    landed(eng, s_w, (u * 2 + r) * LOAD)
                    eng.wait_ge(s_down, free)
                    load(u * 2 + r, r)

        @block.gpsimd
        def _(eng):
            due = eng.alloc_register("due3")
            eng.reg_mov(due, 2)
            def gather(g, r):
                eng.tensor_copy(idx[r][:], io["token"][:, bass.ds(g, 1)]).then_inc(s_idx, 1)
                wait_next(eng, s_idx, due, 1)
                eng.indirect_dma_start(out=x[r][:], out_offset=None, in_=dram["x2"],
                                       in_offset=bass.IndirectOffsetOnAxis(ap=idx[r][:], axis=0)).then_inc(s_x[r], 16)

            def store(g):
                wait(eng, s_y, g + 1)
                eng.dma_start(dram["y"][bass.ts(g, P), :], y[:]).then_inc(s_out, 16)
                landed(eng, s_out, 16 * (g + 1))
                eng.sem_inc(s_kept, 1)

            def body(g, r, u=None):
                if exists(g + 2):
                    wait(eng, s_xt, g + 1)
                    gather(g + 2, r)
                if exists(g - 1):
                    store(g - 1)

            gather(0, 0)
            gather(1, 1)
            tiles(eng, body)
            store(LAST)

        @block.scalar
        def _(eng):
            def turned(g, r):
                wait(eng, s_xt, g + 1)
                eng.activation(xT[r][:], xps[:], ACT.Copy).then_inc(s_xT, 1)

            def body(g, r, u=None):
                wait(eng, s_gate, g + 1)
                if not isinstance(g, int) or g >= 2:
                    wait(eng, s_h, g - 1)
                eng.activation(act[r][:], gate[r][:], ACT.Silu).then_inc(s_act, 1)
                if exists(g + 1):
                    turned(g + 1, 1 - r)

            turned(0, 0)
            tiles(eng, body)

        @block.vector
        def _(eng):
            def turned(g, r):
                wait(eng, s_ht, g + 1)
                for n, (_, size) in enumerate(ICH):
                    ins = eng.tensor_copy(hT[r][0:size, n], hps[0:size, n])
                ins.then_inc(s_hT, 1)

            def result(g):
                wait(eng, s_down, g + 1)
                wait(eng, s_kept, g)
                eng.tensor_copy(y[:], yps[:]).then_inc(s_y, 1)

            def body(g, r, u=None):
                if exists(g - 1):
                    turned(g - 1, 1 - r)
                wait(eng, s_act, g + 1)
                wait(eng, s_up, g + 1)
                eng.tensor_tensor(h[r][:], act[r][:], up[r][:], ALU.mult).then_inc(s_h, 1)
                if exists(g - 1):
                    result(g - 1)

            tiles(eng, body)
            turned(LAST, LAST % 2)
            result(LAST)

        @block.tensor
        def _(eng):
            cell = lambda name, g, most: eng.value_load(io[name][0:1, bass.ds(g, 1)], min_val=0, max_val=most)

            def turn_x(g, r, u):
                landed(eng, s_x[r], 16 * (u + 1))
                for k in range(KD):
                    mm = eng.transpose(xps[:, k, :], x[r][:, k * P:(k + 1) * P], io["ident"])
                mm.then_inc(s_xt, 1)

            def first(g, r, buf, col, out, done):
                for k in range(KD):
                    mm = eng.matmul(out[r][:], xT[r][:, k, :], w13[:, bass.ds(buf, 1), k, col:col + INTER].rearrange("p b n -> p (b n)"),
                                    start=k == 0, stop=k == KD - 1)
                mm.then_inc(done, 1)

            def turn_h(g, r):
                wait(eng, s_h, g + 1)
                for n, (at, size) in enumerate(ICH):
                    mm = eng.transpose(hps[0:size, n, :], h[r][:, at:at + size], io["ident"])
                mm.then_inc(s_ht, 1)

            def down(g, r, buf):
                wait(eng, s_hT, g + 1)
                for n, (_, size) in enumerate(ICH):
                    mm = eng.matmul(yps[:], hT[r][0:size, n, :], w2[0:size, bass.ds(buf, 1), n, :].rearrange("p b n -> p (b n)"),
                                    start=n == 0, stop=n == NI - 1)
                mm.then_inc(s_down, 1)

            def body(g, r, u=None):
                buf = cell("buffer", g, 1)
                landed(eng, s_w, cell("landed", g, LOAD * E))
                wait(eng, s_xT, g + 1)
                if not isinstance(g, int) or g >= 2:
                    wait(eng, s_act, g - 1)
                first(g, r, buf, 0, gate, s_gate)
                if exists(g - 1):
                    turn_h(g - 1, 1 - r)
                first(g, r, buf, INTER, up, s_up)
                if exists(g - 1):
                    down(g - 1, 1 - r, cell("buffer", g - 1, 1))
                if exists(g + 1):
                    after = (g + 1) // 2 if u is None else (u + 1 if r else u)
                    turn_x(g + 1, 1 - r, after)

            turn_x(0, 0, 0)
            tiles(eng, body)
            turn_h(LAST, LAST % 2)
            down(LAST, LAST % 2, cell("buffer", LAST, 1))


def stage_combine(nc, io, dram, out):
    NS = len(SCH)
    with ExitStack() as c:
        sb = lambda n, s, d=F32: c.enter_context(nc.sbuf_tensor(n, s, d))
        ps = lambda n, s: c.enter_context(nc.psum_tensor(n, s, F32))
        sems = []
        dsem = lambda n: c.enter_context(nc.semaphore(n))

        def sem(name):
            sems.append(dsem(name))
            return sems[-1]

        w1, w3, w2 = sb("s_w1", [P, KD, SHARED]), sb("s_w3", [P, KD, SHARED]), sb("s_w2", [P, NS, D])
        xT = sb("s_xT", [P, KD, T])
        act = [sb(f"s_act{i}", [P, SEQ]) for i in range(2)]
        h = sb("s_h", [P, NS, SEQ])
        idx = [sb(f"s_idx{i}", [P, TOPK], I32) for i in range(2)]
        got = [sb(f"s_got{i}", [P, TOPK, D]) for i in range(2)]
        acc = [sb(f"s_acc{i}", [P, D]) for i in range(2)]
        x1, res = sb("s_x1", [P, CH, D]), sb("s_res", [P, CH, D])
        gf, tg = sb("s_gf", [P, 1]), sb("s_tg", [P, 1])
        gate = [ps(f"s_gate{i}", [P, SEQ]) for i in range(2)]
        up = [ps(f"s_up{i}", [P, SEQ]) for i in range(2)]
        yps = [ps(f"s_yps{i}", [P, D]) for i in range(2)]
        s_w, s_w2, s_g, s_x1, s_xT, s_out = (dsem(f"s_s{n}") for n in ("w", "w2", "g", "x1", "xT", "out"))
        s_tg, s_idx, s_link, s_kept = (sem(f"s_s{n}") for n in ("tg", "idx", "link", "kept"))
        s_got = [dsem(f"s_sgot{i}") for i in range(2)]
        s_gu, s_act, s_h, s_dn, s_fin = (sem(f"s_s{n}") for n in ("gu", "act", "h", "dn", "fin"))
        start(nc, sems)
        block = c.enter_context(nc.Block())

        @block.sync
        def _(eng):
            eng.dma_start(xT[:].rearrange("p k (b n) -> p k b n", b=BATCH)[:, :, 0], dram["xT"][0]).then_inc(s_xT, 16)
            eng.dma_start(w1[:], io["ws1T"].rearrange("(c p) n -> p c n", p=P)).then_inc(s_w, 16)
            eng.dma_start(w3[:], io["ws3T"].rearrange("(c p) n -> p c n", p=P)).then_inc(s_w, 16)
            eng.dma_start(gf[:], io["gf"].broadcast_to([P, 1])).then_inc(s_g, 16)
            eng.dma_start(w2[:, 0:NS - 1], io["ws2T"][0:(NS - 1) * P].rearrange("(c p) n -> p c n", p=P)).then_inc(s_w2, 16)
            eng.dma_start(w2[0:SCH[-1][1], NS - 1], io["ws2T"][(NS - 1) * P:SHARED]).then_inc(s_w2, 16)
            for b in range(1, BATCH):
                eng.dma_start(xT[:].rearrange("p k (b n) -> p k b n", b=BATCH)[:, :, b], dram["xT"][b]).then_inc(s_xT, 16)
            with eng.Fori(0, BATCH) as b:
                wait(eng, s_fin, b * CH)
                eng.dma_start(x1[:], dram["x1"][bass.ts(b, SEQ), :].rearrange("(j p) d -> p j d", p=P)).then_inc(s_x1, 16)
                wait(eng, s_fin, (b + 1) * CH)
                eng.dma_start(out[bass.ts(b, SEQ), :].rearrange("(j p) d -> p j d", p=P), res[:]).then_inc(s_out, 16)
                landed(eng, s_out, 16 * (b + 1))
                eng.sem_inc(s_kept, 1)

        @block.gpsimd
        def _(eng):
            due = eng.alloc_register("due4")
            eng.reg_mov(due, 2)
            with eng.Fori(0, BATCH) as b:
                for j in range(CH):
                    wait(eng, s_fin, b * CH + max(0, j - 1))
                    eng.tensor_copy(idx[j % 2][:], io["slot"][:, bass.ds(b * CH + j, 1), :].rearrange("p t k -> p (t k)")).then_inc(s_idx, 1)
                    wait_next(eng, s_idx, due, 1)
                    for k in range(TOPK):
                        eng.indirect_dma_start(out=got[j % 2][:, k, :], out_offset=None, in_=dram["y"],
                                               in_offset=bass.IndirectOffsetOnAxis(ap=idx[j % 2][:, k:k + 1], axis=0)).then_inc(s_got[j % 2], 16)

        @block.scalar
        def _(eng):
            landed(eng, s_g, 16)
            eng.activation(tg[:], gf[:], ACT.Tanh).then_inc(s_tg, 1)
            with eng.Fori(0, BATCH) as b:
                for n, (_, size) in enumerate(SCH):
                    wait(eng, s_gu, b * NS + n + 1)
                    if n >= 2:
                        wait(eng, s_h, b * NS + n - 1)
                    eng.activation(act[n % 2][0:size], gate[n % 2][0:size], ACT.Silu).then_inc(s_act, 1)

        @block.vector
        def _(eng):
            wait(eng, s_tg, 1)
            with eng.Fori(0, BATCH) as b:
                for n, (_, size) in enumerate(SCH):
                    wait(eng, s_act, b * NS + n + 1)
                    eng.tensor_tensor(h[0:size, n, :], act[n % 2][0:size], up[n % 2][0:size], ALU.mult).then_inc(s_h, 1)
                landed(eng, s_x1, 16 * (b + 1))
                wait(eng, s_kept, b)
                for j in range(CH):
                    wait(eng, s_dn, b * CH + j + 1)
                    landed(eng, s_got[j % 2], 16 * TOPK * (b * (CH // 2) + j // 2 + 1))
                    a = acc[j % 2]
                    for k in range(TOPK):
                        w = io["weight"][:, bass.ds(b * CH + j, 1), k]
                        eng.scalar_tensor_tensor(out=a[:], in0=got[j % 2][:, k, :], scalar=w, in1=(a if k else yps[j % 2])[:],
                                                 op0=ALU.mult, op1=ALU.add).then_inc(s_link, 1)
                        wait(eng, s_link, (b * CH + j) * TOPK + k + 1)
                    eng.scalar_tensor_tensor(out=res[:, j, :], in0=a[:], scalar=tg[:, 0:1], in1=x1[:, j, :],
                                             op0=ALU.mult, op1=ALU.add).then_inc(s_fin, 1)

        @block.tensor
        def _(eng):
            due = eng.alloc_register("due5")
            eng.reg_mov(due, NS - 1)
            landed(eng, s_w, 32)
            landed(eng, s_xT, 16 * BATCH)
            landed(eng, s_w2, 32)
            with eng.Fori(0, BATCH) as b:
                for n, (at, size) in enumerate(SCH):
                    if n >= 2:
                        wait_next(eng, s_h, due, NS) if n == NS - 1 else wait(eng, s_h, b * NS + n - 1)
                    for w, bank in ((w1, gate), (w3, up)):
                        for k in range(KD):
                            mm = eng.matmul(bank[n % 2][0:size], w[:, k, at:at + size], xT[:, k, bass.ts(b, SEQ)],
                                            start=k == 0, stop=k == KD - 1)
                    mm.then_inc(s_gu, 1)
                wait(eng, s_h, (b + 1) * NS)
                for j in range(CH):
                    wait(eng, s_link, (b * CH + max(0, j - 1)) * TOPK)
                    for n, (_, size) in enumerate(SCH):
                        mm = eng.matmul(yps[j % 2][:], h[0:size, n, j * P:(j + 1) * P], w2[0:size, n, :], start=n == 0, stop=n == NS - 1)
                    mm.then_inc(s_dn, 1)


def build(nc, ins, out, upto=6):
    dt = lambda n, s, d=F32: nc.dram_tensor(n, s, d).ap()
    dram = {"q": dt("dq", [NIT, 2, 64, SEQ]), "k": dt("dk", [NIT, 2, 2, HD, SEQ]), "v": dt("dv", [NIT, SEQ, VW]),
            "pad": dt("dpad", [NIT, SEQ]), "o": dt("do", [NIT, P, SEQ]),
            "x1": dt("dx1", [T, D]), "x2": dt("dx2", [T, D]), "xT": dt("dxT", [BATCH, P, KD, SEQ]),
            "slots": dt("dslots", [TILES * P, 1]), "y": dt("dy", [TILES * P, D])}
    io = dict(ins)
    with ExitStack() as c:
        sb = lambda n, s, d=F32: c.enter_context(nc.sbuf_tensor(n, s, d))
        for n, d in (("ident", F32), ("identb", BF16), ("late_col", BF16), ("late_row", BF16), ("before", BF16), ("onesb", BF16)):
            io[n] = sb(n, [P, P], d)[:]
        for n, s, d in (("logits", [P, NT, E], F32), ("weight", [P, NT, TOPK], F32), ("slot", [P, NT, TOPK], I32),
                        ("token", [P, TILES], I32), ("expert", [1, TILES], I32), ("buffer", [1, TILES], I32),
                        ("landed", [1, TILES], I32), ("first", [1, E], I32)):
            io[n] = sb(n, s, d)[:]
        stage_constants(nc, io)
        stage_project(nc, io, dram)
        stage_attend(nc, io, dram)
        stage_close(nc, io, dram)
        if upto == 3:
            with nc.semaphore("dbg") as s, nc.Block() as block:
                @block.sync
                def _(eng):
                    eng.dma_start(out, dram["x1"]).then_inc(s, 16)
                    eng.dma_start(io["dbg"], io["logits"].rearrange("p t e -> p (t e)")).then_inc(s, 16)
                    wait(eng, s, 32)
            return
        stage_route(nc, io, dram)
        stage_experts(nc, io, dram)
        stage_combine(nc, io, dram, out)


def layouts(i):
    a = {k: np.asarray(v) for k, v in i.items()}
    qrows = np.arange(D).reshape(GROUPS, HG, HD).transpose(0, 2, 1).ravel()
    t = np.ascontiguousarray
    return {
        "x": a["x"].reshape(T, D), "ctxT": t(a["ctx_2048"].reshape(T, D).T), "mask": a["mask_BxS2_if1"],
        "gx": a["g_xattn"].reshape(1, 1), "gf": a["g_ffn"].reshape(1, 1), "bo": a["L0_xattn_b_o"].reshape(1, D),
        "wqT": t(a["L0_xattn_w_q"][qrows].T), "wkT": t(a["L0_xattn_w_k"].T), "wvT": t(a["L0_xattn_w_v"].T),
        "woT": t(a["L0_xattn_w_o"].T), "wgT": t(a["L0_ffn_Wg"].T),
        "w13T": t(np.concatenate([a["L0_ffn_W1"], a["L0_ffn_W3"]], axis=1).transpose(0, 2, 1)),
        "w2T": t(a["L0_ffn_W2"].transpose(0, 2, 1)),
        "ws1T": t(a["L0_ffn_Ws1"].T), "ws3T": t(a["L0_ffn_Ws3"].T), "ws2T": t(a["L0_ffn_Ws2"].T),
    }


def kernel(**inputs):
    import concourse.bacc as bacc
    from concourse.bass_utils import run_bass_kernel_spmd

    nc = bacc.Bacc("TRN2", target_bir_lowering=False, num_devices=1)
    arrays = {f"in_{n}": a for n, a in layouts(inputs).items()}
    ins = {n[3:]: nc.dram_tensor(n, a.shape, mybir.dt.from_np(a.dtype), kind="ExternalInput").ap() for n, a in arrays.items()}
    out = nc.dram_tensor("out", (T, D), F32, kind="ExternalOutput").ap()
    build(nc, ins, out)
    got = run_bass_kernel_spmd(nc, [arrays], core_ids=[0]).results[0]["out"]
    return got.reshape(BATCH, SEQ, D)
```
